# Optimizing a Trainium2 kernel written in Bass

```python
import numpy as np
import jax
import jax.numpy as jnp

def _softmax(x, axis=-1):
    return jax.nn.softmax(x, axis=axis)

def _gelu(x):
    return jax.nn.gelu(x, approximate=True)

def _silu(x):
    return jax.nn.silu(x)

def _sigmoid(x):
    return jax.nn.sigmoid(x)

def _layernorm(x, axis=-1, eps=1e-05):
    m = jnp.mean(x, axis=axis, keepdims=True)
    v = jnp.var(x, axis=axis, keepdims=True)
    return (x - m) / jnp.sqrt(v + eps)

def _scatter_add(tgt, idx, src, axis=0):
    return tgt.at[idx].add(src)

def _segment_sum(src, seg, n):
    return jax.ops.segment_sum(src, seg, n)
kernel_name = 'mk_adj_resnorm_d2_adj_r2_64f22c'

def setup_inputs(seed: int=0):
    np.random.seed(seed)
    _w = jnp.asarray

    def _rec_inputs():
        import jax
        import jax.numpy as jnp
        _gk = jax.random.key(seed)
        x = -0.0005207 + 1.001 * jax.random.normal(jax.random.fold_in(_gk, 1), (8192, 128), jnp.float32)
        _a = jax.random.bernoulli(jax.random.fold_in(_gk, 2), 0.000488281, (8192, 8192))
        _a = jnp.logical_or(_a, jnp.swapaxes(_a, -1, -2))
        _a = jnp.logical_or(_a, jnp.eye(8192, dtype=bool))
        _af = _a.astype(jnp.float32)
        _af = _af * jax.random.uniform(jax.random.fold_in(_gk, 3), (8192, 8192), jnp.float32, 0.05, 1)
        adj = _af
        return (x, adj)
    x, adj = _rec_inputs()

    def _L0_gnn_setup():
        import jax, jax.numpy as jnp
        import numpy as np
        N, F, OUT = (4096, 128, 128)
        key = jax.random.key(seed)
        k1, k2, k3, k4 = jax.random.split(key, 4)
        features = jax.random.normal(k1, (N, F), dtype=jnp.float32)
        adj = jax.random.uniform(k2, (N, N), dtype=jnp.float32)
        gain = float(np.sqrt(2.0))
        b_n = gain * np.sqrt(6.0 / (F + F))
        neigh_W = jax.random.uniform(k3, (F, F), dtype=jnp.float32, minval=-b_n, maxval=b_n)
        b_l = gain * np.sqrt(6.0 / (2 * F + OUT))
        lin_W = jax.random.uniform(k4, (OUT, 2 * F), dtype=jnp.float32, minval=-b_l, maxval=b_l)
        return {'features': features, 'adj': adj, 'neigh_W': neigh_W, 'lin_W': lin_W}
    _L0_gnn_all = _L0_gnn_setup()
    _L0_gnn_in = {k: v for k, v in _L0_gnn_all.items() if k in ('neigh_W', 'lin_W')}
    del _L0_gnn_all

    def _L1_gnn_setup():
        import jax, jax.numpy as jnp
        import numpy as np
        N_NODES = 8192
        D_FEAT = 128
        key = jax.random.key(seed)
        k1, k2, k3, k4 = jax.random.split(key, 4)
        X = jax.random.normal(k1, (N_NODES, D_FEAT), dtype=jnp.float32)
        A_hat = jax.random.uniform(k2, (N_NODES, N_NODES), dtype=jnp.float32) / N_NODES
        w = jax.random.uniform(k3, (N_NODES,), dtype=jnp.float32)
        W_agg = jax.random.normal(k4, (D_FEAT, D_FEAT), dtype=jnp.float32) / np.sqrt(D_FEAT)
        return {'X': X, 'A_hat': A_hat, 'w': w, 'W_agg': W_agg}
    _L1_gnn_all = _L1_gnn_setup()
    _L1_gnn_in = {k: v for k, v in _L1_gnn_all.items() if k in ('w', 'W_agg')}
    del _L1_gnn_all
    return {'x': x, 'adj': adj, 'L0_gnn_neigh_W': _L0_gnn_in['neigh_W'], 'L0_gnn_lin_W': _L0_gnn_in['lin_W'], 'L1_gnn_w': _L1_gnn_in['w'], 'L1_gnn_W_agg': _L1_gnn_in['W_agg']}

def reference(x, adj, L0_gnn_neigh_W, L0_gnn_lin_W, L1_gnn_w, L1_gnn_W_agg):
    import jax
    import jax.numpy as jnp

    def _L0_gnn_ref(features, adj, neigh_W, lin_W):
        import jax, jax.numpy as jnp
        import numpy as np
        N, F, OUT = (4096, 128, 128)
        h = features @ neigh_W.T
        deg = adj.sum(axis=1, keepdims=True) + 1.0
        h = adj @ h / deg
        z = jnp.concatenate([features, h], axis=-1) @ lin_W.T
        return z

    def _L1_gnn_ref(X, A_hat, w, W_agg):
        import jax, jax.numpy as jnp
        import numpy as np
        N_NODES = 8192
        D_FEAT = 128
        agg = jnp.matmul(jnp.matmul(A_hat, X), W_agg)
        agg = jax.nn.relu(agg)
        s = jax.nn.sigmoid(w)[:, None]
        return s * agg + (1.0 - s) * X
    x = _layernorm(x + _L0_gnn_ref(x, adj, L0_gnn_neigh_W, L0_gnn_lin_W), axis=-1)
    x = _layernorm(x + _L1_gnn_ref(x, adj, L1_gnn_w, L1_gnn_W_agg), axis=-1)
    return x

_drawn_inputs = setup_inputs


def setup_inputs(seed=0):
    import zlib

    import numpy as np

    out = dict(_drawn_inputs(seed))
    spreads = {}
    factors = {}
    for name, (base, spread) in spreads.items():
        noise = np.random.default_rng([zlib.crc32(name.encode()), seed]).standard_normal(out[name].shape)
        drawn = base * np.exp(spread * noise) if base else spread * noise
        out[name] = jnp.asarray(drawn.astype(out[name].dtype))
    for name, factor in factors.items():
        out[name] = (out[name] * factor).astype(out[name].dtype)
    return out
```

```python
from contextlib import ExitStack

import concourse.bass as bass
from concourse import mybir

ALU = mybir.AluOpType
ACT = mybir.ActivationFunctionType
F32 = mybir.dt.float32
F32R = mybir.dt.float32r

P = 128
NODES = 8192
FEAT = 128
LAST = FEAT - 1
BLOCK = 512
CHUNKS = NODES // P
BLOCKS = NODES // BLOCK
SUBS = BLOCK // P
TILE_CHUNKS = 4
TILES = CHUNKS // TILE_CHUNKS
TILE_COLS = TILE_CHUNKS * BLOCK
RING = 4
PIECE_CHUNKS = 2
PIECE_COLS = PIECE_CHUNKS * BLOCK
PIECES = CHUNKS // PIECE_CHUNKS
TILE_PIECES = TILE_CHUNKS // PIECE_CHUNKS
HI_BUFS = 4
LO_BUFS = 2
QUARTERS = NODES // TILE_COLS
QUARTER_BANKS = TILE_COLS // BLOCK
EPS = 1e-5
PEELED = 3

ACT_STEPS = {4: "copy sums", 8: "part", 16: "std", 22: "x1 hi"}
PE_TURN = 3
DVE_STEPS = {6: "prepare", 9: "y", 10: "stats", 11: "moments", 17: "normalise", 23: "x1 lo"}


def graph_two_layers(nc, adj_tiles, xT, neigh_W, lin_WT, w_nodes, W_agg, out):
    with ExitStack() as ctx:
        def sb(name, shape, dt=F32):
            return ctx.enter_context(nc.sbuf_tensor(name, shape, dt))

        def bank(name):
            return ctx.enter_context(nc.psum_tensor(name, [P, BLOCK], F32))

        def sem(name):
            return ctx.enter_context(nc.semaphore(name))

        ring = sb("ring", [P, RING, TILE_COLS])
        adj_hi = sb("adj_hi", [P, HI_BUFS, PIECE_COLS], F32R)
        adj_lo = sb("adj_lo", [P, LO_BUFS, PIECE_COLS], F32R)
        h_hi = sb("h_hi", [P, CHUNKS, FEAT], F32R)
        h_lo = sb("h_lo", [P, CHUNKS, FEAT], F32R)
        x1_hi = sb("x1_hi", [P, CHUNKS, FEAT], F32R)
        x1_lo = sb("x1_lo", [P, CHUNKS, FEAT], F32R)
        x_block = sb("x_block", [P, 2, BLOCK])
        neigh_w = sb("neigh_w", [P, FEAT])
        lin_w = sb("lin_w", [P, 2, FEAT])
        agg_w = sb("agg_w", [P, FEAT])
        w_sb = sb("w_sb", [P, CHUNKS])
        ident = sb("ident", [P, FEAT])
        g_raw = sb("g_raw", [P, FEAT])
        g_shift = sb("g_shift", [P, FEAT])
        self_w = sb("self_w", [P, FEAT])
        gate = sb("gate", [P, CHUNKS])
        keep = sb("keep", [P, CHUNKS])
        sumT = sb("sumT", [P, BLOCK])
        part = sb("part", [P, SUBS, FEAT])
        resid = sb("resid", [P, SUBS, FEAT])
        y = sb("y", [P, SUBS, FEAT])
        normed = sb("normed", [P, 2, SUBS, FEAT])
        eps = sb("eps", [P, 1])
        inv_deg = sb("inv_deg", [P, SUBS])
        deg1 = sb("deg1", [P, SUBS])
        stats = sb("stats", [P, SUBS, 6])
        moments = sb("moments", [P, SUBS, 2])
        std = sb("std", [P, SUBS])
        rstd = sb("rstd", [P, SUBS])

        acc = [bank("acc0"), bank("acc1")]
        self_ps = bank("self_ps")
        turned = bank("turned")
        h_ps = [bank(f"h_ps{n}") for n in range(QUARTER_BANKS)]
        self_v = self_ps[:, :].rearrange("p (s f) -> p s f", s=SUBS)
        turned_v = turned[:, :].rearrange("p (s f) -> p s f", s=SUBS)

        weights_in = sem("weights_in")
        quarter_in = [sem(f"quarter_in{q}") for q in range(QUARTERS)]
        tile_in = [sem(f"tile_in{r}") for r in range(RING)]
        xblock_in = [sem(f"xblock_in{r}") for r in range(2)]
        out_done = [sem(f"out_done{r}") for r in range(2)]
        ident_zero = sem("ident_zero")
        ident_made = sem("ident_made")
        ones_made = sem("ones_made")
        eps_made = sem("eps_made")
        g_summed = sem("g_summed")
        g_copied = sem("g_copied")
        g_shifted = sem("g_shifted")
        self_made = sem("self_made")
        gate_made = sem("gate_made")
        keep_made = sem("keep_made")
        h_summed = sem("h_summed")
        h_hi_made = sem("h_hi_made")
        h_lo_made = sem("h_lo_made")
        hi_made = sem("hi_made")
        lo_made = sem("lo_made")
        piece_used = sem("piece_used")
        sum_copied = sem("sum_copied")
        turned_made = sem("turned_made")
        part_made = sem("part_made")
        deg_made = sem("deg_made")
        inv_made = sem("inv_made")
        resid_made = sem("resid_made")
        y_made = sem("y_made")
        stats_made = sem("stats_made")
        moments_made = sem("moments_made")
        std_made = sem("std_made")
        rstd_made = sem("rstd_made")
        normed_made = sem("normed_made")
        x1_hi_made = sem("x1_hi_made")
        x1_lo_made = sem("x1_lo_made")

        def all_blocks(engine, step):
            for layer in range(2):
                first = layer * BLOCKS
                for n in range(PEELED):
                    step(layer, first + n, n % 2)
                with engine.Fori(0, (BLOCKS - 1 - PEELED) // 2) as pair:
                    step(layer, pair * 2 + (first + PEELED), 1)
                    step(layer, pair * 2 + (first + PEELED + 1), 0)
                step(layer, first + BLOCKS - 1, 1)

        def is_first(blk):
            return isinstance(blk, int) and blk == 0

        def layer_before(layer, blk):
            return 0 if isinstance(blk, int) and blk == BLOCKS else layer

        block = ctx.enter_context(nc.Block())

        @block.sync
        def _(sp):
            sp.dma_start(neigh_w[:, :], neigh_W).then_inc(weights_in, 16)
            sp.dma_start(lin_w[:, :, :], lin_WT).then_inc(weights_in, 16)
            for q in range(QUARTERS):
                sp.dma_start(ring[:, q, :], xT[:, q * TILE_COLS:(q + 1) * TILE_COLS]).then_inc(quarter_in[q], 16)
            sp.dma_start(agg_w[:, :], W_agg).then_inc(weights_in, 16)
            sp.dma_start(w_sb[:, :], w_nodes).then_inc(weights_in, 16)

            def load_block(layer, blk, parity):
                target = blk - layer * BLOCKS
                if layer == 0:
                    if not isinstance(blk, int) or blk >= 2:
                        sp.wait_ge(turned_made, blk - 1)
                    sp.dma_start(x_block[:, parity, :], xT[:, bass.ds(target * BLOCK, BLOCK)]).then_inc(xblock_in[parity], 16)
                for t in range(TILES):
                    if is_first(blk) and t < RING:
                        sp.wait_ge(h_summed, (t + 1) * QUARTER_BANKS)
                    else:
                        sp.wait_ge(lo_made, blk * PIECES + TILE_PIECES * (t - RING + 1))
                    sp.dma_start(ring[:, t % RING, :], adj_tiles[target * TILES + t, :, :]).then_inc(tile_in[t % RING], 16)
            all_blocks(sp, load_block)

        @block.gpsimd
        def _(pool):
            nc.gpsimd.memset(ident[:, :], 0.0).then_inc(ident_zero, 1)
            nc.gpsimd.memset(eps[:, :], EPS).then_inc(eps_made, 1)
            nc.gpsimd.memset(h_hi[:, :, LAST:FEAT].bitcast(F32), 1.0)
            nc.gpsimd.memset(h_lo[:, :, LAST:FEAT].bitcast(F32), 0.0).then_inc(ones_made, 1)
            pool.wait_ge(ident_zero, 1)
            nc.gpsimd.affine_select(out=ident[:, :], in_=ident[:, :], compare_op=ALU.not_equal, fill=1.0, base=0,
                                    pattern=[[-1, FEAT]], channel_multiplier=1).then_inc(ident_made, 1)

            def store_block(blk, parity):
                pool.wait_ge(normed_made, blk + 1)
                target = blk - BLOCKS
                pool.dma_start(out[:, bass.ds(target * SUBS, SUBS), :], normed[:, parity, :, :]).then_inc(out_done[parity], 16)
            with pool.Fori(0, BLOCKS // 2) as pair:
                store_block(pair * 2 + BLOCKS, 0)
                store_block(pair * 2 + (BLOCKS + 1), 1)
            for r in range(2):
                pool.wait_ge(out_done[r], 16 * (BLOCKS // 2))

        @block.scalar
        def _(act):
            act.wait_ge(g_summed, 1)
            nc.scalar.copy(g_raw[:, :], turned[:, 0:FEAT]).then_inc(g_copied, 1)
            for c in range(CHUNKS // SUBS):
                act.wait_ge(h_summed, c + 1)
                src = h_ps[c % QUARTER_BANKS][:, :].rearrange("p (s f) -> p s f", s=SUBS)
                nc.scalar.copy(h_hi[:, c * SUBS:(c + 1) * SUBS, 0:LAST], src[:, :, 0:LAST]).then_inc(h_hi_made, 1)
            act.wait_ge(weights_in, 64)
            nc.scalar.activation(gate[:, :], w_sb[:, :], ACT.Sigmoid).then_inc(gate_made, 1)
            act.wait_ge(eps_made, 1)

            def finish(layer, blk, parity, step):
                if step == "copy sums":
                    act.wait_ge(piece_used, blk * PIECES + PIECES)
                    if not is_first(blk):
                        act.wait_ge(turned_made, blk)
                    nc.scalar.copy(sumT[:, :], acc[parity][:, :]).then_inc(sum_copied, 1)
                elif step == "part":
                    act.wait_ge(turned_made, blk + 1)
                    if not is_first(blk):
                        act.wait_ge(y_made, blk)
                    if layer == 0:
                        nc.scalar.copy(part[:, :, :], self_v[:, :, :]).then_inc(part_made, 1)
                    else:
                        for s in range(SUBS):
                            node_chunk = (blk - BLOCKS) * SUBS + s
                            done = nc.scalar.activation(part[:, s, :], turned_v[:, s, :], ACT.Relu,
                                                        scale=gate[:, bass.ds(node_chunk, 1)])
                        done.then_inc(part_made, 1)
                elif step == "std":
                    act.wait_ge(moments_made, blk + 1)
                    nc.scalar.activation(std[:, :], moments[:, :, 1], ACT.Sqrt, bias=eps[:, :]).then_inc(std_made, 1)
                elif step == "x1 hi" and layer == 0:
                    act.wait_ge(normed_made, blk + 1)
                    nc.scalar.copy(x1_hi[:, bass.ds(blk * SUBS, SUBS), :], normed[:, parity, :, :]).then_inc(x1_hi_made, 1)

            def split_block(layer, blk, parity):
                for j in range(PIECES):
                    t, half = j // TILE_PIECES, j % TILE_PIECES
                    if half == 0:
                        act.wait_ge(tile_in[t % RING], blk * (16 * TILES // RING) + 16 * (t // RING + 1))
                    if not is_first(blk) or j >= HI_BUFS:
                        act.wait_ge(piece_used, blk * PIECES + (j - HI_BUFS + 1))
                    nc.scalar.copy(adj_hi[:, j % HI_BUFS, :],
                                   ring[:, t % RING, half * PIECE_COLS:(half + 1) * PIECE_COLS]).then_inc(hi_made, 1)
                    if not is_first(blk) and j in ACT_STEPS:
                        finish(layer_before(layer, blk), blk - 1, 1 - parity, ACT_STEPS[j])
            all_blocks(act, split_block)
            for step in ACT_STEPS.values():
                finish(1, 2 * BLOCKS - 1, 1, step)

        @block.vector
        def _(dve):
            dve.wait_ge(g_copied, 1)
            nc.vector.tensor_scalar(g_shift[:, :], g_raw[:, :], g_raw[:, LAST:FEAT], None, ALU.subtract).then_inc(g_shifted, 1)
            dve.wait_ge(ident_made, 1)
            dve.wait_ge(weights_in, 64)
            nc.vector.tensor_tensor(self_w[:, :], lin_w[:, 0, :], ident[:, :], ALU.add).then_inc(self_made, 1)
            for c in range(CHUNKS // SUBS):
                dve.wait_ge(h_hi_made, c + 1)
                src = h_ps[c % QUARTER_BANKS][:, :].rearrange("p (s f) -> p s f", s=SUBS)
                cols = slice(c * SUBS, (c + 1) * SUBS)
                nc.vector.tensor_tensor(h_lo[:, cols, 0:LAST], src[:, :, 0:LAST],
                                        h_hi[:, cols, 0:LAST].bitcast(F32), ALU.subtract).then_inc(h_lo_made, 1)
            dve.wait_ge(gate_made, 1)
            nc.vector.tensor_scalar(keep[:, :], gate[:, :], -1.0, 2.0, ALU.mult, ALU.add).then_inc(keep_made, 1)

            def finish(layer, blk, parity, step):
                if step == "prepare" and layer == 0:
                    dve.wait_ge(turned_made, blk + 1)
                    nc.vector.tensor_scalar(deg1[:, :], turned_v[:, :, LAST], 1.0, None, ALU.add).then_inc(deg_made, 1)
                    dve.wait_ge(deg_made, blk + 1)
                    nc.vector.reciprocal(inv_deg[:, :], deg1[:, :]).then_inc(inv_made, 1)
                elif step == "prepare":
                    if isinstance(blk, int) and blk == BLOCKS:
                        dve.wait_ge(x1_lo_made, BLOCKS)
                        dve.wait_ge(keep_made, 1)
                    cols = bass.ds((blk - BLOCKS) * SUBS, SUBS)
                    nc.vector.tensor_tensor(resid[:, :, :], x1_hi[:, cols, :].bitcast(F32),
                                            x1_lo[:, cols, :].bitcast(F32), ALU.add).then_inc(resid_made, 1)
                elif step == "y" and layer == 0:
                    dve.wait_ge(part_made, blk + 1)
                    dve.wait_ge(inv_made, blk + 1)
                    for s in range(SUBS):
                        nc.vector.scalar_tensor_tensor(out=y[:, s, 0:LAST], in0=turned_v[:, s, 0:LAST],
                                                       scalar=inv_deg[:, s:s + 1], in1=part[:, s, 0:LAST],
                                                       op0=ALU.mult, op1=ALU.add)
                    nc.vector.tensor_copy(y[:, :, LAST:FEAT], part[:, :, LAST:FEAT]).then_inc(y_made, 1)
                elif step == "y":
                    dve.wait_ge(part_made, blk + 1)
                    dve.wait_ge(resid_made, blk - BLOCKS + 1)
                    for s in range(SUBS):
                        node_chunk = (blk - BLOCKS) * SUBS + s
                        done = nc.vector.scalar_tensor_tensor(out=y[:, s, :], in0=resid[:, s, :],
                                                              scalar=keep[:, bass.ds(node_chunk, 1)], in1=part[:, s, :],
                                                              op0=ALU.mult, op1=ALU.add)
                    done.then_inc(y_made, 1)
                elif step == "stats":
                    dve.wait_ge(y_made, blk + 1)
                    for s in range(SUBS):
                        done = nc.vector.bn_stats(stats[:, s, :], y[:, s, :])
                    done.then_inc(stats_made, 1)
                elif step == "moments":
                    for s in range(SUBS):
                        done = nc.vector.bn_aggr(moments[:, s, :], stats[:, s, :])
                    done.then_inc(moments_made, 1)
                elif step == "normalise":
                    dve.wait_ge(std_made, blk + 1)
                    nc.vector.reciprocal(rstd[:, :], std[:, :]).then_inc(rstd_made, 1)
                    dve.wait_ge(rstd_made, blk + 1)
                    if layer == 1 and (not isinstance(blk, int) or blk >= BLOCKS + 2):
                        dve.wait_ge(out_done[parity], (blk - BLOCKS - parity) * 8)
                    for s in range(SUBS):
                        done = nc.vector.tensor_scalar(normed[:, parity, s, :], y[:, s, :], moments[:, s, 0:1],
                                                       rstd[:, s:s + 1], ALU.subtract, ALU.mult)
                    done.then_inc(normed_made, 1)
                elif step == "x1 lo" and layer == 0:
                    dve.wait_ge(x1_hi_made, blk + 1)
                    cols = bass.ds(blk * SUBS, SUBS)
                    nc.vector.tensor_tensor(x1_lo[:, cols, :], normed[:, parity, :, :],
                                            x1_hi[:, cols, :].bitcast(F32), ALU.subtract).then_inc(x1_lo_made, 1)

            def split_block(layer, blk, parity):
                for j in range(PIECES):
                    t, half = j // TILE_PIECES, j % TILE_PIECES
                    dve.wait_ge(hi_made, blk * PIECES + (j + 1))
                    if not is_first(blk) or j >= LO_BUFS:
                        dve.wait_ge(piece_used, blk * PIECES + (j - LO_BUFS + 1))
                    if not is_first(blk) and DVE_STEPS.get(j) == "moments":
                        dve.wait_ge(stats_made, blk)
                    nc.vector.tensor_tensor(adj_lo[:, j % LO_BUFS, :],
                                            ring[:, t % RING, half * PIECE_COLS:(half + 1) * PIECE_COLS],
                                            adj_hi[:, j % HI_BUFS, :].bitcast(F32), ALU.subtract).then_inc(lo_made, 1)
                    if not is_first(blk) and j in DVE_STEPS:
                        finish(layer_before(layer, blk), blk - 1, 1 - parity, DVE_STEPS[j])
            all_blocks(dve, split_block)
            for step in DVE_STEPS.values():
                if step == "moments":
                    dve.wait_ge(stats_made, 2 * BLOCKS)
                finish(1, 2 * BLOCKS - 1, 1, step)

        @block.tensor
        def _(pe):
            pe.wait_ge(weights_in, 64)
            nc.tensor.matmul(turned[:, 0:FEAT], neigh_w[:, :], lin_w[:, 1, :], start=True, stop=True).then_inc(g_summed, 1)
            pe.wait_ge(g_shifted, 1)
            for c in range(CHUNKS // SUBS):
                if c % QUARTER_BANKS == 0:
                    pe.wait_ge(quarter_in[c // QUARTER_BANKS], 16)
                if c >= QUARTER_BANKS:
                    pe.wait_ge(h_lo_made, c - QUARTER_BANKS + 1)
                for s in range(SUBS):
                    at = (c % QUARTER_BANKS) * BLOCK + s * P
                    done = nc.tensor.matmul(h_ps[c % QUARTER_BANKS][:, s * FEAT:(s + 1) * FEAT],
                                            ring[:, c // QUARTER_BANKS, at:at + P], g_shift[:, :], start=True, stop=True)
                done.then_inc(h_summed, 1)
            pe.wait_ge(ones_made, 1)
            pe.wait_ge(self_made, 1)

            def finish(layer, blk, parity):
                pe.wait_ge(sum_copied, blk + 1)
                if not is_first(blk):
                    pe.wait_ge(y_made, blk)
                if layer == 0:
                    pe.wait_ge(xblock_in[parity], (blk - parity) * 8 + 16)
                    for s in range(SUBS):
                        nc.tensor.matmul(self_v[:, s, :], x_block[:, parity, s * P:(s + 1) * P], self_w[:, :],
                                         start=True, stop=True)
                for s in range(SUBS):
                    done = nc.tensor.matmul(turned_v[:, s, :], sumT[:, s * P:(s + 1) * P],
                                            ident[:, :] if layer == 0 else agg_w[:, :], start=True, stop=True)
                done.then_inc(turned_made, 1)

            def sum_block(layer, blk, parity):
                feat_hi, feat_lo = (h_hi, h_lo) if layer == 0 else (x1_hi, x1_lo)
                for j in range(PIECES):
                    if is_first(blk) and j % (SUBS // PIECE_CHUNKS) == 0:
                        pe.wait_ge(h_lo_made, j * PIECE_CHUNKS // SUBS + 1)
                    if isinstance(blk, int) and blk == BLOCKS and j * PIECE_CHUNKS % SUBS == 0:
                        pe.wait_ge(x1_lo_made, j * PIECE_CHUNKS // SUBS + 1)
                    if j == 0 and not (isinstance(blk, int) and blk < 2):
                        pe.wait_ge(sum_copied, blk - 1)
                    pe.wait_ge(hi_made, blk * PIECES + (j + 1))
                    for k in range(PIECE_CHUNKS):
                        chunk = j * PIECE_CHUNKS + k
                        hi = adj_hi[:, j % HI_BUFS, k * BLOCK:(k + 1) * BLOCK]
                        nc.tensor.matmul(acc[parity][:, :], feat_hi[:, chunk, :], hi, start=(chunk == 0), stop=False)
                        nc.tensor.matmul(acc[parity][:, :], feat_lo[:, chunk, :], hi, start=False, stop=False)
                    pe.wait_ge(lo_made, blk * PIECES + (j + 1))
                    for k in range(PIECE_CHUNKS):
                        chunk = j * PIECE_CHUNKS + k
                        done = nc.tensor.matmul(acc[parity][:, :], feat_hi[:, chunk, :],
                                                adj_lo[:, j % LO_BUFS, k * BLOCK:(k + 1) * BLOCK],
                                                start=False, stop=(chunk == CHUNKS - 1))
                    done.then_inc(piece_used, 1)
                    if j == PE_TURN and not is_first(blk):
                        finish(layer_before(layer, blk), blk - 1, 1 - parity)
            all_blocks(pe, sum_block)
            finish(1, 2 * BLOCKS - 1, 1)


def kernel(x, adj, L0_gnn_neigh_W, L0_gnn_lin_W, L1_gnn_w, L1_gnn_W_agg):
    import numpy as np
    import concourse.bacc as bacc
    from concourse.bass_utils import run_bass_kernel_spmd

    adj = np.asarray(adj)
    tiles = adj.reshape(BLOCKS, BLOCK, TILES, TILE_CHUNKS, P).transpose(0, 2, 4, 3, 1)
    arrays = {
        "adj_tiles": np.ascontiguousarray(tiles).reshape(BLOCKS * TILES, P, TILE_COLS),
        "xT": np.ascontiguousarray(np.asarray(x).T),
        "neigh_W": np.ascontiguousarray(L0_gnn_neigh_W),
        "lin_WT": np.ascontiguousarray(np.asarray(L0_gnn_lin_W).T.reshape(2, FEAT, FEAT).transpose(1, 0, 2)),
        "w_nodes": np.ascontiguousarray(np.asarray(L1_gnn_w).reshape(CHUNKS, P).T),
        "W_agg": np.ascontiguousarray(L1_gnn_W_agg),
    }
    nc = bacc.Bacc("TRN2", target_bir_lowering=False, num_devices=1)
    args = [nc.dram_tensor(name, a.shape, mybir.dt.from_np(a.dtype), kind="ExternalInput").ap()
            for name, a in arrays.items()]
    out = nc.dram_tensor("out", (P, CHUNKS, FEAT), F32, kind="ExternalOutput").ap()
    graph_two_layers(nc, *args, out)
    r = run_bass_kernel_spmd(nc, [arrays], core_ids=[0])
    return np.ascontiguousarray(r.results[0]["out"].transpose(1, 0, 2)).reshape(NODES, FEAT)
```

```python
from contextlib import ExitStack

import concourse.bass as bass
from concourse import mybir

ALU = mybir.AluOpType
ACT = mybir.ActivationFunctionType
F32 = mybir.dt.float32
F32R = mybir.dt.float32r

P = 128
NODES = 8192
FEAT = 128
LAST = FEAT - 1
BLOCK = 512
CHUNKS = NODES // P
BLOCKS = NODES // BLOCK
SUBS = BLOCK // P
TILE_CHUNKS = SUBS
TILES = CHUNKS // TILE_CHUNKS
TILE_COLS = TILE_CHUNKS * BLOCK
RING = 4
PIECE_CHUNKS = 2
PIECE_COLS = PIECE_CHUNKS * BLOCK
TILE_PIECES = TILE_CHUNKS // PIECE_CHUNKS
HI_BUFS = 4
LO_BUFS = 2
QUARTERS = NODES // TILE_COLS
BANK_CHUNKS = 2
H_FILLS = CHUNKS // BANK_CHUNKS
QUARTER_FILLS = H_FILLS // QUARTERS
H_BANKS = 3
EPS = 1e-5

MOST_SHARED = 8
GROUPS = [(b, b + 1, b) for b in range(MOST_SHARED)] + [(MOST_SHARED, BLOCKS, MOST_SHARED)]
FIRST_SHARING = 1
LOOP_FIRST = MOST_SHARED

ACT_STEPS = {4: "copy sums", 6: "copy partial", 8: "part", 14: "std", 18: "x1 hi"}
PE_TURN = 1
DVE_STEPS = {1: "add partial", 2: "residual", 3: "inverse", 4: "y", 5: "moments", 7: "normalise", 9: "x1 lo"}
PARTIAL_LOAD = 6


def graph_two_layers(nc, adj_tiles, xT, neigh_W, lin_WT, w_nodes, W_agg, partials, out):
    with ExitStack() as ctx:
        def sb(name, shape, dt=F32):
            return ctx.enter_context(nc.sbuf_tensor(name, shape, dt))

        def bank(name):
            return ctx.enter_context(nc.psum_tensor(name, [P, BLOCK], F32))

        def sem(name):
            return ctx.enter_context(nc.semaphore(name))

        ring = sb("ring", [P, RING, TILE_COLS])
        adj_hi = sb("adj_hi", [P, HI_BUFS, PIECE_COLS], F32R)
        adj_lo = sb("adj_lo", [P, LO_BUFS, TILE_COLS], F32R)
        h_hi = sb("h_hi", [P, CHUNKS, FEAT], F32R)
        h_lo = sb("h_lo", [P, CHUNKS, FEAT], F32R)
        x1_hi = sb("x1_hi", [P, CHUNKS, FEAT], F32R)
        x1_lo = sb("x1_lo", [P, CHUNKS, FEAT], F32R)
        neigh_w = sb("neigh_w", [P, FEAT])
        lin_w = sb("lin_w", [P, 2, FEAT])
        agg_w = sb("agg_w", [P, FEAT])
        w_sb = sb("w_sb", [P, CHUNKS])
        ident = sb("ident", [P, FEAT])
        g_raw = sb("g_raw", [P, FEAT])
        first_w = sb("first_w", [P, 2, FEAT])
        gate = sb("gate", [P, CHUNKS])
        keep = sb("keep", [P, CHUNKS])
        sumT = sb("sumT", [P, BLOCK])
        partial_out = sb("partial_out", [P, BLOCK])
        partial_in = sb("partial_in", [P, BLOCK])
        part = sb("part", [P, SUBS, FEAT])
        y = sb("y", [P, SUBS, FEAT])
        eps = sb("eps", [P, 1])
        inv_deg = sb("inv_deg", [P, SUBS])
        deg1 = sb("deg1", [P, SUBS])
        stats = sb("stats", [P, SUBS, 6])
        moments = sb("moments", [P, SUBS, 2])
        std = sb("std", [P, SUBS])
        rstd = sb("rstd", [P, SUBS])

        acc = [bank("acc0"), bank("acc1")]
        acc_partial = bank("acc_partial")
        turned = bank("turned")
        h_ps = [bank(f"h_ps{n}") for n in range(H_BANKS)]
        turned_v = turned[:, :].rearrange("p (s f) -> p s f", s=SUBS)

        weights_in = sem("weights_in")
        late_in = sem("late_in")
        quarter_in = [sem(f"quarter_in{q}") for q in range(QUARTERS)]
        tile_in = [sem(f"tile_in{r}") for r in range(RING)]
        partial_stored = sem("partial_stored")
        partial_loaded = sem("partial_loaded")
        out_done = sem("out_done")
        ident_zero = sem("ident_zero")
        ident_made = sem("ident_made")
        ones_made = sem("ones_made")
        eps_made = sem("eps_made")
        g_summed = sem("g_summed")
        g_copied = sem("g_copied")
        g_shifted = sem("g_shifted")
        self_made = sem("self_made")
        gate_made = sem("gate_made")
        keep_made = sem("keep_made")
        h_summed = sem("h_summed")
        h_hi_made = sem("h_hi_made")
        h_lo_made = sem("h_lo_made")
        hi_made = sem("hi_made")
        lo_made = sem("lo_made")
        hi_used = sem("hi_used")
        tile_used = sem("tile_used")
        sum_copied = sem("sum_copied")
        sum_added = sem("sum_added")
        partial_copied = sem("partial_copied")
        turned_made = sem("turned_made")
        part_made = sem("part_made")
        deg_made = sem("deg_made")
        inv_made = sem("inv_made")
        residual_made = sem("residual_made")
        y_made = sem("y_made")
        stats_made = sem("stats_made")
        moments_made = sem("moments_made")
        std_made = sem("std_made")
        rstd_made = sem("rstd_made")
        normed_made = sem("normed_made")
        x1_hi_made = sem("x1_hi_made")
        x1_lo_made = sem("x1_lo_made")

        def all_blocks(engine, step):
            for layer in range(2):
                for first, end, shared in GROUPS:
                    if first < LOOP_FIRST:
                        for b in range(first, end):
                            step(layer, b, shared, b % 2)
                    else:
                        with engine.Fori(0, (end - first) // 2) as pair:
                            step(layer, pair * 2 + first, shared, 0)
                            step(layer, pair * 2 + (first + 1), shared, 1)

        def before(layer, b):
            if isinstance(b, int) and b == 0:
                return None if layer == 0 else (0, BLOCKS - 1)
            return layer, b - 1

        def number(layer, b):
            return b + layer * BLOCKS if layer else b

        def shares(b):
            return not isinstance(b, int) or b >= FIRST_SHARING

        def tile_order(layer, shared):
            return list(range(shared, TILES)) + (list(range(shared)) if layer == 0 else [])

        def tiles_before(layer, b, shared, per=1):
            if layer == 0:
                return b * (TILES // per)
            done = BLOCKS * TILES
            for first, end, s in GROUPS:
                if s == shared:
                    break
                done += (end - first) * (TILES - s)
            return b * ((TILES - shared) // per) + (done - first * (TILES - shared)) // per

        def buffer_of(layer, b, shared, n, count, per=1):
            done = tiles_before(layer, b, shared) if isinstance(b, int) else 0
            return (done * per + n) % count

        def slot_loads(layer, b, shared, t):
            if isinstance(b, int):
                return (tiles_before(layer, b, shared) + t) // RING + 1
            return tiles_before(layer, b, shared, RING) + (t // RING + 1)

        block = ctx.enter_context(nc.Block())

        @block.sync
        def _(sp):
            sp.dma_start(neigh_w[:, :], neigh_W).then_inc(weights_in, 16)
            sp.dma_start(lin_w[:, :, :], lin_WT).then_inc(weights_in, 16)
            for q in range(QUARTERS):
                sp.dma_start(ring[:, q, :], xT[:, q * TILE_COLS:(q + 1) * TILE_COLS]).then_inc(quarter_in[q], 16)
            sp.dma_start(agg_w[:, :], W_agg).then_inc(late_in, 16)
            sp.dma_start(w_sb[:, :], w_nodes).then_inc(late_in, 16)

            def load_block(layer, b, shared, parity):
                if layer == 1 and isinstance(b, int) and b == FIRST_SHARING:
                    sp.wait_ge(partial_stored, 16 * (BLOCKS - FIRST_SHARING))
                for t, tile in enumerate(tile_order(layer, shared)):
                    if before(layer, b) is None and t < RING:
                        sp.wait_ge(h_summed, (t + 1) * QUARTER_FILLS)
                    else:
                        sp.wait_ge(lo_made, tiles_before(layer, b, shared) + (t - RING + 1))
                    slot = buffer_of(layer, b, shared, t, RING)
                    sp.dma_start(ring[:, slot, :], adj_tiles[b * TILES + tile, :, :]).then_inc(tile_in[slot], 16)
                    if layer == 1 and shares(b) and t == PARTIAL_LOAD:
                        sp.wait_ge(sum_added, b)
                        sp.dma_start(partial_in[:, :], partials[b - FIRST_SHARING, :, :]).then_inc(partial_loaded, 16)
            all_blocks(sp, load_block)

        @block.gpsimd
        def _(pool):
            nc.gpsimd.memset(ident[:, :], 0.0).then_inc(ident_zero, 1)
            nc.gpsimd.memset(eps[:, :], EPS).then_inc(eps_made, 1)
            nc.gpsimd.memset(h_hi[:, :, LAST:FEAT].bitcast(F32), 1.0)
            nc.gpsimd.memset(h_lo[:, :, LAST:FEAT].bitcast(F32), 0.0).then_inc(ones_made, 1)
            pool.wait_ge(ident_zero, 1)
            nc.gpsimd.affine_select(out=ident[:, :], in_=ident[:, :], compare_op=ALU.not_equal, fill=1.0, base=0,
                                    pattern=[[-1, FEAT]], channel_multiplier=1).then_inc(ident_made, 1)

            with pool.Fori(0, BLOCKS - FIRST_SHARING) as n:
                pool.wait_ge(partial_copied, n + 1)
                pool.dma_start(partials[n, :, :], partial_out[:, :]).then_inc(partial_stored, 16)
            pool.wait_ge(partial_stored, 16 * (BLOCKS - FIRST_SHARING))

            with pool.Fori(0, BLOCKS) as b:
                pool.wait_ge(normed_made, b + (BLOCKS + 1))
                pool.dma_start(out[:, bass.ds(b * SUBS, SUBS), :], y[:, :, :]).then_inc(out_done, 16)
            pool.wait_ge(out_done, 16 * BLOCKS)

        @block.scalar
        def _(act):
            act.wait_ge(g_summed, 1)
            nc.scalar.copy(g_raw[:, :], turned[:, 0:FEAT]).then_inc(g_copied, 1)
            for c in range(H_FILLS):
                act.wait_ge(h_summed, c + 1)
                src = h_ps[c % H_BANKS][:, :].rearrange("p (c w f) -> p c w f", c=BANK_CHUNKS, w=2)
                chunks = slice(c * BANK_CHUNKS, (c + 1) * BANK_CHUNKS)
                nc.scalar.copy(h_hi[:, chunks, 0:LAST], src[:, :, 0, 0:LAST])
                nc.scalar.copy(x1_hi[:, chunks, :], src[:, :, 1, :]).then_inc(h_hi_made, 1)
            act.wait_ge(late_in, 32)
            nc.scalar.activation(gate[:, :], w_sb[:, :], ACT.Sigmoid).then_inc(gate_made, 1)
            act.wait_ge(eps_made, 1)

            def finish(layer, b, step, tiles_done):
                n = number(layer, b)
                if step == "copy sums" and layer == 0:
                    act.wait_ge(tile_used, tiles_done)
                    if not (isinstance(b, int) and b == 0):
                        act.wait_ge(turned_made, n)
                    nc.scalar.copy(sumT[:, :], acc_of(b)[:, :]).then_inc(sum_copied, 1)
                elif step == "copy partial" and layer == 0 and shares(b):
                    if not (isinstance(b, int) and b == FIRST_SHARING):
                        act.wait_ge(partial_stored, (b - FIRST_SHARING) * 16)
                    nc.scalar.copy(partial_out[:, :], acc_partial[:, :]).then_inc(partial_copied, 1)
                elif step == "part" and layer == 1:
                    act.wait_ge(turned_made, n + 1)
                    for s in range(SUBS):
                        done = nc.scalar.activation(part[:, s, :], turned_v[:, s, :], ACT.Relu,
                                                    scale=gate[:, bass.ds(b * SUBS + s, 1)])
                    done.then_inc(part_made, 1)
                elif step == "std":
                    act.wait_ge(moments_made, n + 1)
                    nc.scalar.activation(std[:, :], moments[:, :, 1], ACT.Sqrt, bias=eps[:, :]).then_inc(std_made, 1)
                elif step == "x1 hi" and layer == 0:
                    act.wait_ge(normed_made, n + 1)
                    nc.scalar.copy(x1_hi[:, bass.ds(b * SUBS, SUBS), :], y[:, :, :]).then_inc(x1_hi_made, 1)

            parity_now = [0]

            def acc_of(b):
                return acc[1 - parity_now[0]]

            def round_block(layer, b, shared, parity):
                parity_now[0] = parity
                tiles_done = tiles_before(layer, b, shared)
                for j in range(len(tile_order(layer, shared)) * TILE_PIECES):
                    t, half = j // TILE_PIECES, j % TILE_PIECES
                    slot = buffer_of(layer, b, shared, t, RING)
                    if half == 0:
                        act.wait_ge(tile_in[slot], slot_loads(layer, b, shared, t) * 16)
                    if before(layer, b) is not None or j >= HI_BUFS:
                        act.wait_ge(hi_used, tiles_done * TILE_PIECES + (j - HI_BUFS + 1))
                        if half == 0:
                            act.wait_ge(lo_made, tiles_done + (t - HI_BUFS // TILE_PIECES + 1))
                    nc.scalar.copy(adj_hi[:, buffer_of(layer, b, shared, j, HI_BUFS, TILE_PIECES), :],
                                   ring[:, slot, half * PIECE_COLS:(half + 1) * PIECE_COLS]).then_inc(hi_made, 1)
                    if before(layer, b) is not None and j in ACT_STEPS:
                        finish(*before(layer, b), ACT_STEPS[j], tiles_done)
            all_blocks(act, round_block)
            for step in ACT_STEPS.values():
                finish(1, BLOCKS - 1, step, None)

        @block.vector
        def _(dve):
            dve.wait_ge(g_copied, 1)
            nc.vector.tensor_scalar(first_w[:, 0, :], g_raw[:, :], g_raw[:, LAST:FEAT], None, ALU.subtract).then_inc(g_shifted, 1)
            dve.wait_ge(ident_made, 1)
            dve.wait_ge(weights_in, 32)
            nc.vector.tensor_tensor(first_w[:, 1, :], lin_w[:, 0, :], ident[:, :], ALU.add).then_inc(self_made, 1)
            for c in range(H_FILLS):
                dve.wait_ge(h_hi_made, c + 1)
                src = h_ps[c % H_BANKS][:, :].rearrange("p (c w f) -> p c w f", c=BANK_CHUNKS, w=2)
                chunks = slice(c * BANK_CHUNKS, (c + 1) * BANK_CHUNKS)
                nc.vector.tensor_tensor(h_lo[:, chunks, 0:LAST], src[:, :, 0, 0:LAST],
                                        h_hi[:, chunks, 0:LAST].bitcast(F32), ALU.subtract)
                nc.vector.tensor_tensor(x1_lo[:, chunks, :], src[:, :, 1, :],
                                        x1_hi[:, chunks, :].bitcast(F32), ALU.subtract).then_inc(h_lo_made, 1)
            dve.wait_ge(gate_made, 1)
            nc.vector.tensor_scalar(keep[:, :], gate[:, :], -1.0, 2.0, ALU.mult, ALU.add).then_inc(keep_made, 1)
            dve.wait_ge(keep_made, 1)

            def finish(layer, b, parity, step, tiles_done):
                n = number(layer, b)
                nodes = bass.ds(b * SUBS, SUBS)
                if step == "add partial" and layer == 1:
                    dve.wait_ge(tile_used, tiles_done)
                    dve.wait_ge(turned_made, n)
                    if shares(b):
                        dve.wait_ge(partial_loaded, (b - FIRST_SHARING + 1) * 16)
                        nc.vector.tensor_tensor(sumT[:, :], acc[parity][:, :], partial_in[:, :], ALU.add).then_inc(sum_added, 1)
                    else:
                        nc.vector.tensor_copy(sumT[:, :], acc[parity][:, :]).then_inc(sum_added, 1)
                elif step == "residual":
                    if layer == 0 and isinstance(b, int) and b == 0:
                        dve.wait_ge(h_lo_made, H_FILLS)
                    if layer == 1 and isinstance(b, int) and b == 0:
                        dve.wait_ge(x1_lo_made, BLOCKS)
                    elif layer == 1:
                        dve.wait_ge(out_done, b * 16)
                    nc.vector.tensor_tensor(y[:, :, :], x1_hi[:, nodes, :].bitcast(F32),
                                            x1_lo[:, nodes, :].bitcast(F32), ALU.add).then_inc(residual_made, 1)
                elif step == "inverse" and layer == 0:
                    dve.wait_ge(turned_made, n + 1)
                    nc.vector.tensor_scalar(deg1[:, :], turned_v[:, :, LAST], 1.0, None, ALU.add).then_inc(deg_made, 1)
                    dve.wait_ge(deg_made, b + 1)
                    nc.vector.reciprocal(inv_deg[:, :], deg1[:, :]).then_inc(inv_made, 1)
                elif step == "y":
                    dve.wait_ge(residual_made, n + 1)
                    if layer == 0:
                        dve.wait_ge(inv_made, b + 1)
                        for s in range(SUBS):
                            done = nc.vector.scalar_tensor_tensor(out=y[:, s, 0:LAST], in0=turned_v[:, s, 0:LAST],
                                                                  scalar=inv_deg[:, s:s + 1], in1=y[:, s, 0:LAST],
                                                                  op0=ALU.mult, op1=ALU.add)
                    else:
                        dve.wait_ge(part_made, b + 1)
                        for s in range(SUBS):
                            done = nc.vector.scalar_tensor_tensor(out=y[:, s, :], in0=y[:, s, :],
                                                                  scalar=keep[:, bass.ds(b * SUBS + s, 1)],
                                                                  in1=part[:, s, :], op0=ALU.mult, op1=ALU.add)
                    done.then_inc(y_made, 1)
                    dve.wait_ge(y_made, n + 1)
                    for s in range(SUBS):
                        done = nc.vector.bn_stats(stats[:, s, :], y[:, s, :])
                    done.then_inc(stats_made, 1)
                elif step == "moments":
                    for s in range(SUBS):
                        done = nc.vector.bn_aggr(moments[:, s, :], stats[:, s, :])
                    done.then_inc(moments_made, 1)
                elif step == "normalise":
                    dve.wait_ge(std_made, n + 1)
                    nc.vector.reciprocal(rstd[:, :], std[:, :]).then_inc(rstd_made, 1)
                    dve.wait_ge(rstd_made, n + 1)
                    for s in range(SUBS):
                        done = nc.vector.tensor_scalar(y[:, s, :], y[:, s, :], moments[:, s, 0:1],
                                                       rstd[:, s:s + 1], ALU.subtract, ALU.mult)
                    done.then_inc(normed_made, 1)
                elif step == "x1 lo" and layer == 0:
                    dve.wait_ge(x1_hi_made, b + 1)
                    nc.vector.tensor_tensor(x1_lo[:, nodes, :], y[:, :, :],
                                            x1_hi[:, nodes, :].bitcast(F32), ALU.subtract).then_inc(x1_lo_made, 1)

            def split_block(layer, b, shared, parity):
                tiles_done = tiles_before(layer, b, shared)
                for t in range(len(tile_order(layer, shared))):
                    hi_at = buffer_of(layer, b, shared, t * TILE_PIECES, HI_BUFS, TILE_PIECES)
                    step = DVE_STEPS.get(t) if before(layer, b) is not None else None
                    dve.wait_ge(hi_made, (tiles_done + (t + 1)) * TILE_PIECES)
                    if before(layer, b) is not None or t >= LO_BUFS:
                        dve.wait_ge(tile_used, tiles_done + (t - LO_BUFS + 1))
                    if step == "moments":
                        dve.wait_ge(stats_made, number(layer, b))
                    nc.vector.tensor_tensor(adj_lo[:, buffer_of(layer, b, shared, t, LO_BUFS), :],
                                            ring[:, buffer_of(layer, b, shared, t, RING), :],
                                            adj_hi[:, hi_at:hi_at + TILE_PIECES, :].bitcast(F32).rearrange("p a n -> p (a n)"),
                                            ALU.subtract).then_inc(lo_made, 1)
                    if step is not None:
                        finish(*before(layer, b), 1 - parity, step, tiles_done)
            all_blocks(dve, split_block)
            for step in DVE_STEPS.values():
                if step == "moments":
                    dve.wait_ge(stats_made, 2 * BLOCKS)
                finish(1, BLOCKS - 1, 1, step, ALL_TILES)

        @block.tensor
        def _(pe):
            pe.wait_ge(weights_in, 32)
            nc.tensor.matmul(turned[:, 0:FEAT], neigh_w[:, :], lin_w[:, 1, :], start=True, stop=True).then_inc(g_summed, 1)
            pe.wait_ge(g_shifted, 1)
            pe.wait_ge(self_made, 1)
            for c in range(H_FILLS):
                if c % QUARTER_FILLS == 0:
                    pe.wait_ge(quarter_in[c // QUARTER_FILLS], 16)
                if c >= H_BANKS:
                    pe.wait_ge(h_lo_made, c - H_BANKS + 1)
                for s in range(BANK_CHUNKS):
                    at = (c % QUARTER_FILLS) * BANK_CHUNKS * P + s * P
                    done = nc.tensor.matmul(h_ps[c % H_BANKS][:, s * 2 * FEAT:(s + 1) * 2 * FEAT],
                                            ring[:, c // QUARTER_FILLS, at:at + P],
                                            first_w[:, :, :].rearrange("p w f -> p (w f)"), start=True, stop=True)
                done.then_inc(h_summed, 1)
            pe.wait_ge(ones_made, 1)

            def finish(layer, b):
                n = number(layer, b)
                if layer == 0:
                    pe.wait_ge(sum_copied, b + 1)
                else:
                    pe.wait_ge(sum_added, b + 1)
                if isinstance(b, int) and b == 0 and layer == 1:
                    pe.wait_ge(late_in, 32)
                if not (isinstance(b, int) and b == 0 and layer == 0):
                    pe.wait_ge(y_made, n)
                for s in range(SUBS):
                    if layer == 0:
                        done = nc.tensor.transpose(turned_v[:, s, :], sumT[:, s * P:(s + 1) * P], ident[:, :])
                    else:
                        done = nc.tensor.matmul(turned_v[:, s, :], sumT[:, s * P:(s + 1) * P], agg_w[:, :],
                                                start=True, stop=True)
                done.then_inc(turned_made, 1)

            def sum_block(layer, b, shared, parity):
                tiles_done = tiles_before(layer, b, shared)
                order = tile_order(layer, shared)
                if not isinstance(b, int) or b >= 2:
                    pe.wait_ge(sum_added if layer else sum_copied, b - 1)
                elif layer == 1:
                    pe.wait_ge(sum_copied, BLOCKS - 1 + b)
                for t, tile in enumerate(order):
                    feats = [(acc[parity], *((x1_hi, x1_lo) if layer else (h_hi, h_lo)), t == 0, t == len(order) - 1)]
                    if layer == 0 and tile < shared:
                        feats.append((acc_partial, x1_hi, x1_lo, tile == 0, tile == shared - 1))
                        if tile == 0 or tile == shared - 1:
                            pe.wait_ge(x1_lo_made, shared if tile == shared - 1 else shared - 1)
                        if tile == 0:
                            if not (isinstance(b, int) and b == FIRST_SHARING):
                                pe.wait_ge(partial_copied, b - FIRST_SHARING)
                    if layer == 1 and isinstance(b, int) and b == 0 and tile in (0, TILES - 1):
                        pe.wait_ge(x1_lo_made, BLOCKS - 1 if tile == 0 else BLOCKS)
                    for half in range(TILE_PIECES):
                        j = t * TILE_PIECES + half
                        hi_buf = buffer_of(layer, b, shared, j, HI_BUFS, TILE_PIECES)
                        chunk = tile * TILE_CHUNKS + half * PIECE_CHUNKS
                        if before(layer, b) is None:
                            pe.wait_ge(h_lo_made, (chunk + PIECE_CHUNKS) // BANK_CHUNKS)
                        pe.wait_ge(hi_made, tiles_done * TILE_PIECES + (j + 1))
                        for bank_, feat_hi, feat_lo, first, _ in feats:
                            for k in range(PIECE_CHUNKS):
                                hi = adj_hi[:, hi_buf, k * BLOCK:(k + 1) * BLOCK]
                                nc.tensor.matmul(bank_[:, :], feat_hi[:, chunk + k, :], hi,
                                                 start=(first and half + k == 0), stop=False)
                                done = nc.tensor.matmul(bank_[:, :], feat_lo[:, chunk + k, :], hi, start=False, stop=False)
                        done.then_inc(hi_used, 1)
                    pe.wait_ge(lo_made, tiles_done + (t + 1))
                    lo_buf = buffer_of(layer, b, shared, t, LO_BUFS)
                    for bank_, feat_hi, _, _, last in feats:
                        for k in range(TILE_CHUNKS):
                            done = nc.tensor.matmul(bank_[:, :], feat_hi[:, tile * TILE_CHUNKS + k, :],
                                                    adj_lo[:, lo_buf, k * BLOCK:(k + 1) * BLOCK], start=False,
                                                    stop=(last and k == TILE_CHUNKS - 1))
                    done.then_inc(tile_used, 1)
                    if t == PE_TURN and before(layer, b) is not None:
                        finish(*before(layer, b))
            all_blocks(pe, sum_block)
            finish(1, BLOCKS - 1)


ALL_TILES = sum((end - first) * (2 * TILES - shared) for first, end, shared in GROUPS)


def kernel(x, adj, L0_gnn_neigh_W, L0_gnn_lin_W, L1_gnn_w, L1_gnn_W_agg):
    import numpy as np
    import concourse.bacc as bacc
    from concourse.bass_utils import run_bass_kernel_spmd

    adj = np.asarray(adj)
    tiles = adj.reshape(BLOCKS, BLOCK, TILES, TILE_CHUNKS, P).transpose(0, 2, 4, 3, 1)
    arrays = {
        "adj_tiles": np.ascontiguousarray(tiles).reshape(BLOCKS * TILES, P, TILE_COLS),
        "xT": np.ascontiguousarray(np.asarray(x).T),
        "neigh_W": np.ascontiguousarray(L0_gnn_neigh_W),
        "lin_WT": np.ascontiguousarray(np.asarray(L0_gnn_lin_W).T.reshape(2, FEAT, FEAT).transpose(1, 0, 2)),
        "w_nodes": np.ascontiguousarray(np.asarray(L1_gnn_w).reshape(CHUNKS, P).T),
        "W_agg": np.ascontiguousarray(L1_gnn_W_agg),
    }
    nc = bacc.Bacc("TRN2", target_bir_lowering=False, num_devices=1)
    args = [nc.dram_tensor(name, a.shape, mybir.dt.from_np(a.dtype), kind="ExternalInput").ap()
            for name, a in arrays.items()]
    partials = nc.dram_tensor("partials", (BLOCKS - FIRST_SHARING, P, BLOCK), F32).ap()
    out = nc.dram_tensor("out", (P, CHUNKS, FEAT), F32, kind="ExternalOutput").ap()
    graph_two_layers(nc, *args, partials, out)
    r = run_bass_kernel_spmd(nc, [arrays], core_ids=[0])
    return np.ascontiguousarray(r.results[0]["out"].transpose(1, 0, 2)).reshape(NODES, FEAT)
```

```python
from contextlib import ExitStack

import concourse.bass as bass
from concourse import mybir

ALU = mybir.AluOpType
ACT = mybir.ActivationFunctionType
F32 = mybir.dt.float32
F32R = mybir.dt.float32r

P = 128
NODES = 8192
FEAT = 128
LAST = FEAT - 1
BLOCK = 512
CHUNKS = NODES // P
BLOCKS = NODES // BLOCK
SUBS = BLOCK // P
TILE_CHUNKS = SUBS
TILES = CHUNKS // TILE_CHUNKS
TILE_COLS = TILE_CHUNKS * BLOCK
RING = 4
LATE_SLOTS = 4
PIECE_CHUNKS = 2
PIECE_COLS = PIECE_CHUNKS * BLOCK
TILE_PIECES = TILE_CHUNKS // PIECE_CHUNKS
HI_BUFS = 4
LO_BUFS = 2
QUARTERS = NODES // TILE_COLS
BANK_CHUNKS = 2
H_FILLS = CHUNKS // BANK_CHUNKS
QUARTER_FILLS = H_FILLS // QUARTERS
H_BANKS = 5
EPS = 1e-5

MOST_SHARED = 8
GROUPS = [(b, b + 1, b) for b in range(MOST_SHARED)] + [(MOST_SHARED, BLOCKS, MOST_SHARED)]
FIRST_SHARING = 1
LOOP_FIRST = MOST_SHARED

ACT_STEPS = {4: "copy sums", 6: "copy partial", 8: "part", 14: "std", 18: "x1 hi"}
PE_TURN = 1
DVE_STEPS = {1: "add partial", 2: "residual", 3: "inverse", 4: "y", 5: "moments", 7: "normalise", 9: "x1 lo"}
PARTIAL_LOAD = 6


def graph_two_layers(nc, adj_tiles, xT, neigh_W, lin_WT, w_nodes, W_agg, partials, out):
    with ExitStack() as ctx:
        def sb(name, shape, dt=F32):
            return ctx.enter_context(nc.sbuf_tensor(name, shape, dt))

        def bank(name):
            return ctx.enter_context(nc.psum_tensor(name, [P, BLOCK], F32))

        def sem(name):
            return ctx.enter_context(nc.semaphore(name))

        ring = sb("ring", [P, RING, TILE_COLS])
        with nc.sbuf_tensor("x_cols", [P, QUARTERS, TILE_COLS], F32) as x_cols:
            pass
        adj_hi = sb("adj_hi", [P, HI_BUFS, PIECE_COLS], F32R)
        adj_lo = sb("adj_lo", [P, LO_BUFS, TILE_COLS], F32R)
        with nc.sbuf_tensor("h_first_half", [P, CHUNKS // 2, 2, FEAT], F32):
            with nc.sbuf_tensor("late_ring", [P, LATE_SLOTS, TILE_COLS], F32) as late_ring:
                pass
        h = sb("h", [P, CHUNKS, 2, FEAT], F32R)
        h_hi, h_lo = h[:, :, 0, :], h[:, :, 1, :]
        x1_hi = sb("x1_hi", [P, CHUNKS, FEAT], F32R)
        x1_lo = sb("x1_lo", [P, CHUNKS, FEAT], F32R)
        agg_w = sb("agg_w", [P, FEAT])
        w_sb = sb("w_sb", [P, CHUNKS])
        ident = sb("ident", [P, FEAT])
        first_w = sb("first_w", [P, 2, FEAT])
        gate = sb("gate", [P, CHUNKS])
        keep = sb("keep", [P, CHUNKS])
        sumT = sb("sumT", [P, BLOCK])
        stage = sb("stage", [P, SUBS, FEAT])
        with nc.sbuf_tensor("setup", [P, 4, FEAT], F32) as setup:
            pass
        neigh_w = setup[:, 0, :]
        lin_w = setup[:, 1:3, :]
        g_raw = setup[:, 3, :]
        partial_in = sb("partial_in", [P, 2, BLOCK])
        part = sb("part", [P, SUBS, FEAT])
        y = sb("y", [P, SUBS, FEAT])
        eps = sb("eps", [P, 1])
        inv_deg = sb("inv_deg", [P, SUBS])
        deg1 = sb("deg1", [P, SUBS])
        stats = sb("stats", [P, SUBS, 6])
        moments = sb("moments", [P, SUBS, 2])
        std = sb("std", [P, SUBS])
        rstd = sb("rstd", [P, SUBS])

        acc = [bank("acc0"), bank("acc1")]
        acc_partial = bank("acc_partial")
        turned = bank("turned")
        h_ps = [bank(f"h_ps{n}") for n in range(H_BANKS - 2)] + [acc[1], acc_partial]
        stage_flat = stage[:, :, :].rearrange("p s f -> p (s f)")
        turned_v = turned[:, :].rearrange("p (s f) -> p s f", s=SUBS)

        weights_in = sem("weights_in")
        agg_w_in = sem("agg_w_in")
        quarter_in = [sem(f"quarter_in{q}") for q in range(QUARTERS)]
        tile_in = [sem(f"tile_in{r}") for r in range(RING + LATE_SLOTS)]
        w_in = sem("w_in")
        partial_stored = sem("partial_stored")
        partial_loaded = [sem(f"partial_loaded{r}") for r in range(2)]
        out_done = sem("out_done")
        last_out_done = sem("last_out_done")
        ident_zero = sem("ident_zero")
        ident_made = sem("ident_made")
        ones_made = sem("ones_made")
        eps_made = sem("eps_made")
        g_summed = sem("g_summed")
        g_copied = sem("g_copied")
        g_shifted = sem("g_shifted")
        self_made = sem("self_made")
        gate_made = sem("gate_made")
        keep_made = sem("keep_made")
        h_summed = sem("h_summed")
        h_hi_made = sem("h_hi_made")
        h_lo_made = sem("h_lo_made")
        hi_made = sem("hi_made")
        lo_made = sem("lo_made")
        hi_used = sem("hi_used")
        tile_used = sem("tile_used")
        sum_copied = sem("sum_copied")
        sum_added = sem("sum_added")
        partial_copied = sem("partial_copied")
        turned_made = sem("turned_made")
        part_made = sem("part_made")
        deg_made = sem("deg_made")
        inv_made = sem("inv_made")
        residual_made = sem("residual_made")
        y_made = sem("y_made")
        stats_made = sem("stats_made")
        moments_made = sem("moments_made")
        std_made = sem("std_made")
        rstd_made = sem("rstd_made")
        normed_made = sem("normed_made")
        x1_hi_made = sem("x1_hi_made")
        x1_lo_made = sem("x1_lo_made")

        def all_blocks(engine, step):
            for layer in range(2):
                for first, end, shared in GROUPS:
                    if first < LOOP_FIRST:
                        for b in range(first, end):
                            step(layer, b, shared, b % 2)
                    else:
                        with engine.Fori(0, (end - first) // 2) as pair:
                            step(layer, pair * 2 + first, shared, 0)
                            step(layer, pair * 2 + (first + 1), shared, 1)

        def before(layer, b):
            if isinstance(b, int) and b == 0:
                return None if layer == 0 else (0, BLOCKS - 1)
            return layer, b - 1

        def number(layer, b):
            return b + layer * BLOCKS if layer else b

        def shares(b):
            return not isinstance(b, int) or b >= FIRST_SHARING

        def tile_order(layer, shared):
            return list(range(shared, TILES)) + (list(range(shared)) if layer == 0 else [])

        def tiles_before(layer, b, shared):
            if layer == 0:
                return b * TILES
            done = BLOCKS * TILES
            for first, end, s in GROUPS:
                if s == shared:
                    break
                done += (end - first) * (TILES - s)
            return b * (TILES - shared) + (done - first * (TILES - shared))

        def known_before(layer, b, shared):
            return tiles_before(layer, b if isinstance(b, int) else LOOP_FIRST, shared)

        def buffer_of(layer, b, shared, n, count, per=1):
            return (known_before(layer, b, shared) * per + n) % count

        def slot_of(layer, b, shared, t):
            slots = RING + LATE_SLOTS * layer
            at = known_before(layer, b, shared) + t - layer * BLOCKS * TILES
            slot = at % slots
            memory = ring[:, slot, :] if slot < RING else late_ring[:, slot - RING, :]
            loads = at // slots + 1 + (BLOCKS * TILES // RING if layer and slot < RING else 0)
            if not isinstance(b, int):
                blocks_loads = (TILES if layer == 0 else TILES - shared) // slots
                loads = b * blocks_loads + (loads - LOOP_FIRST * blocks_loads)
            return slot, memory, loads

        block = ctx.enter_context(nc.Block())

        @block.sync
        def _(sp):
            sp.dma_start(neigh_w[:, :], neigh_W).then_inc(weights_in, 16)
            sp.dma_start(lin_w[:, :, :], lin_WT).then_inc(weights_in, 16)
            sp.dma_start(w_sb[:, :], w_nodes).then_inc(w_in, 16)
            for q in range(QUARTERS):
                sp.dma_start(x_cols[:, q, :], xT[:, q * TILE_COLS:(q + 1) * TILE_COLS]).then_inc(quarter_in[q], 16)
            sp.dma_start(agg_w[:, :], W_agg).then_inc(agg_w_in, 16)

            def load_block(layer, b, shared, parity):
                if layer == 1 and isinstance(b, int) and b == FIRST_SHARING:
                    sp.wait_ge(partial_stored, 16 * (BLOCKS - FIRST_SHARING))
                for t, tile in enumerate(tile_order(layer, shared)):
                    slot, memory, _ = slot_of(layer, b, shared, t)
                    if layer == 1 and isinstance(b, int) and b == 0 and RING <= t < RING + LATE_SLOTS:
                        sp.wait_ge(tile_used, (BLOCKS - 1) * TILES + TILES // 2)
                    elif not (before(layer, b) is None and t < RING):
                        back = RING if layer == 0 or (isinstance(b, int) and b == 0 and t < RING) else RING + LATE_SLOTS
                        sp.wait_ge(lo_made, tiles_before(layer, b, shared) + (t - back + 1))
                    sp.dma_start(memory, adj_tiles[b * TILES + tile, :, :]).then_inc(tile_in[slot], 16)
                    if layer == 1 and shares(b) and t == PARTIAL_LOAD:
                        if not isinstance(b, int) or b >= FIRST_SHARING + 2:
                            sp.wait_ge(sum_added, b - 1)
                        sp.dma_start(partial_in[:, parity, :], partials[b - FIRST_SHARING, :, :]).then_inc(partial_loaded[parity], 16)
            all_blocks(sp, load_block)

            sp.wait_ge(normed_made, 2 * BLOCKS)
            sp.dma_start(out[:, (BLOCKS - 1) * SUBS:, :], stage[:, :, :]).then_inc(last_out_done, 16)
            sp.wait_ge(last_out_done, 16)

        @block.gpsimd
        def _(pool):
            nc.gpsimd.memset(ident[:, :], 0.0).then_inc(ident_zero, 1)
            nc.gpsimd.memset(eps[:, :], EPS).then_inc(eps_made, 1)
            nc.gpsimd.memset(h_hi[:, :, LAST:FEAT].bitcast(F32), 1.0)
            nc.gpsimd.memset(h_lo[:, :, LAST:FEAT].bitcast(F32), 0.0).then_inc(ones_made, 1)
            pool.wait_ge(ident_zero, 1)
            nc.gpsimd.affine_select(out=ident[:, :], in_=ident[:, :], compare_op=ALU.not_equal, fill=1.0, base=0,
                                    pattern=[[-1, FEAT]], channel_multiplier=1).then_inc(ident_made, 1)

            with pool.Fori(0, BLOCKS - FIRST_SHARING) as n:
                pool.wait_ge(partial_copied, n + 1)
                pool.dma_start(partials[n, :, :], stage_flat).then_inc(partial_stored, 16)
            pool.wait_ge(partial_stored, 16 * (BLOCKS - FIRST_SHARING))

            with pool.Fori(0, BLOCKS - 1) as b:
                pool.wait_ge(normed_made, b + (BLOCKS + 1))
                pool.dma_start(out[:, bass.ds(b * SUBS, SUBS), :], stage[:, :, :]).then_inc(out_done, 16)
            pool.wait_ge(out_done, 16 * (BLOCKS - 1))

        @block.scalar
        def _(act):
            act.wait_ge(w_in, 16)
            nc.scalar.activation(gate[:, :], w_sb[:, :], ACT.Sigmoid).then_inc(gate_made, 1)
            act.wait_ge(g_summed, 1)
            nc.scalar.copy(g_raw[:, :], turned[:, 0:FEAT]).then_inc(g_copied, 1)
            for c in range(H_FILLS):
                act.wait_ge(h_summed, c + 1)
                src = h_ps[c % H_BANKS][:, :].rearrange("p (c w f) -> p c w f", c=BANK_CHUNKS, w=2)
                chunks = slice(c * BANK_CHUNKS, (c + 1) * BANK_CHUNKS)
                nc.scalar.copy(h_hi[:, chunks, 0:LAST], src[:, :, 0, 0:LAST])
                nc.scalar.copy(x1_hi[:, chunks, :], src[:, :, 1, :]).then_inc(h_hi_made, 1)
            act.wait_ge(eps_made, 1)

            def finish(layer, b, parity, step, tiles_done):
                n = number(layer, b)
                if step == "copy sums" and layer == 0:
                    act.wait_ge(tile_used, tiles_done)
                    if not (isinstance(b, int) and b == 0):
                        act.wait_ge(turned_made, n)
                    nc.scalar.copy(sumT[:, :], acc[parity][:, :]).then_inc(sum_copied, 1)
                elif step == "copy partial" and layer == 0 and shares(b):
                    if not (isinstance(b, int) and b == FIRST_SHARING):
                        act.wait_ge(partial_stored, (b - FIRST_SHARING) * 16)
                    nc.scalar.copy(stage_flat, acc_partial[:, :]).then_inc(partial_copied, 1)
                elif step == "part" and layer == 1:
                    act.wait_ge(turned_made, n + 1)
                    for s in range(SUBS):
                        done = nc.scalar.activation(part[:, s, :], turned_v[:, s, :], ACT.Relu,
                                                    scale=gate[:, bass.ds(b * SUBS + s, 1)])
                    done.then_inc(part_made, 1)
                elif step == "std":
                    act.wait_ge(moments_made, n + 1)
                    nc.scalar.activation(std[:, :], moments[:, :, 1], ACT.Sqrt, bias=eps[:, :]).then_inc(std_made, 1)
                elif step == "x1 hi" and layer == 0:
                    act.wait_ge(normed_made, n + 1)
                    nc.scalar.copy(x1_hi[:, bass.ds(b * SUBS, SUBS), :], y[:, :, :]).then_inc(x1_hi_made, 1)

            def round_block(layer, b, shared, parity):
                tiles_done = tiles_before(layer, b, shared)
                for j in range(len(tile_order(layer, shared)) * TILE_PIECES):
                    t, half = j // TILE_PIECES, j % TILE_PIECES
                    slot, memory, loads = slot_of(layer, b, shared, t)
                    if half == 0:
                        act.wait_ge(tile_in[slot], loads * 16)
                    if before(layer, b) is not None or j >= HI_BUFS:
                        act.wait_ge(hi_used, tiles_done * TILE_PIECES + (j - HI_BUFS + 1))
                        if half == 0:
                            act.wait_ge(lo_made, tiles_done + (t - HI_BUFS // TILE_PIECES + 1))
                    nc.scalar.copy(adj_hi[:, buffer_of(layer, b, shared, j, HI_BUFS, TILE_PIECES), :],
                                   memory[:, half * PIECE_COLS:(half + 1) * PIECE_COLS]).then_inc(hi_made, 1)
                    if before(layer, b) is not None and j in ACT_STEPS:
                        finish(*before(layer, b), 1 - parity, ACT_STEPS[j], tiles_done)
            all_blocks(act, round_block)
            for step in ACT_STEPS.values():
                finish(1, BLOCKS - 1, 1, step, ALL_TILES)

        @block.vector
        def _(dve):
            dve.wait_ge(g_copied, 1)
            nc.vector.tensor_scalar(first_w[:, 0, :], g_raw[:, :], g_raw[:, LAST:FEAT], None, ALU.subtract).then_inc(g_shifted, 1)
            dve.wait_ge(ident_made, 1)
            dve.wait_ge(weights_in, 32)
            nc.vector.tensor_tensor(first_w[:, 1, :], lin_w[:, 0, :], ident[:, :], ALU.add).then_inc(self_made, 1)
            for c in range(H_FILLS):
                dve.wait_ge(h_hi_made, c + 1)
                src = h_ps[c % H_BANKS][:, :].rearrange("p (c w f) -> p c w f", c=BANK_CHUNKS, w=2)
                chunks = slice(c * BANK_CHUNKS, (c + 1) * BANK_CHUNKS)
                nc.vector.tensor_tensor(h_lo[:, chunks, 0:LAST], src[:, :, 0, 0:LAST],
                                        h_hi[:, chunks, 0:LAST].bitcast(F32), ALU.subtract)
                nc.vector.tensor_tensor(x1_lo[:, chunks, :], src[:, :, 1, :],
                                        x1_hi[:, chunks, :].bitcast(F32), ALU.subtract).then_inc(h_lo_made, 1)
            dve.wait_ge(gate_made, 1)
            nc.vector.tensor_scalar(keep[:, :], gate[:, :], -1.0, 2.0, ALU.mult, ALU.add).then_inc(keep_made, 1)
            dve.wait_ge(keep_made, 1)

            def finish(layer, b, parity, step, tiles_done):
                n = number(layer, b)
                nodes = bass.ds(b * SUBS, SUBS)
                if step == "add partial" and layer == 1:
                    dve.wait_ge(tile_used, tiles_done)
                    dve.wait_ge(turned_made, n)
                    if shares(b):
                        dve.wait_ge(partial_loaded[parity], (b + parity) * 8)
                        nc.vector.tensor_tensor(sumT[:, :], acc[parity][:, :], partial_in[:, parity, :], ALU.add).then_inc(sum_added, 1)
                    else:
                        nc.vector.tensor_copy(sumT[:, :], acc[parity][:, :]).then_inc(sum_added, 1)
                elif step == "residual":
                    if layer == 0 and isinstance(b, int) and b == 0:
                        dve.wait_ge(h_lo_made, H_FILLS)
                    if layer == 1 and isinstance(b, int) and b == 0:
                        dve.wait_ge(x1_lo_made, BLOCKS)
                    if not (layer == 0 and isinstance(b, int) and b == 0):
                        dve.wait_ge(normed_made, n)
                    nc.vector.tensor_tensor(y[:, :, :], x1_hi[:, nodes, :].bitcast(F32),
                                            x1_lo[:, nodes, :].bitcast(F32), ALU.add).then_inc(residual_made, 1)
                elif step == "inverse" and layer == 0:
                    dve.wait_ge(turned_made, n + 1)
                    nc.vector.tensor_scalar(deg1[:, :], turned_v[:, :, LAST], 1.0, None, ALU.add).then_inc(deg_made, 1)
                    dve.wait_ge(deg_made, b + 1)
                    nc.vector.reciprocal(inv_deg[:, :], deg1[:, :]).then_inc(inv_made, 1)
                elif step == "y":
                    dve.wait_ge(residual_made, n + 1)
                    if layer == 0:
                        dve.wait_ge(inv_made, b + 1)
                        for s in range(SUBS):
                            done = nc.vector.scalar_tensor_tensor(out=y[:, s, 0:LAST], in0=turned_v[:, s, 0:LAST],
                                                                  scalar=inv_deg[:, s:s + 1], in1=y[:, s, 0:LAST],
                                                                  op0=ALU.mult, op1=ALU.add)
                    else:
                        dve.wait_ge(part_made, b + 1)
                        for s in range(SUBS):
                            done = nc.vector.scalar_tensor_tensor(out=y[:, s, :], in0=y[:, s, :],
                                                                  scalar=keep[:, bass.ds(b * SUBS + s, 1)],
                                                                  in1=part[:, s, :], op0=ALU.mult, op1=ALU.add)
                    done.then_inc(y_made, 1)
                    dve.wait_ge(y_made, n + 1)
                    for s in range(SUBS):
                        done = nc.vector.bn_stats(stats[:, s, :], y[:, s, :])
                    done.then_inc(stats_made, 1)
                elif step == "moments":
                    for s in range(SUBS):
                        done = nc.vector.bn_aggr(moments[:, s, :], stats[:, s, :])
                    done.then_inc(moments_made, 1)
                elif step == "normalise":
                    dve.wait_ge(std_made, n + 1)
                    nc.vector.reciprocal(rstd[:, :], std[:, :]).then_inc(rstd_made, 1)
                    dve.wait_ge(rstd_made, n + 1)
                    if layer == 1 and isinstance(b, int) and b == 0:
                        dve.wait_ge(partial_stored, 16 * (BLOCKS - FIRST_SHARING))
                    elif layer == 1:
                        dve.wait_ge(out_done, b * 16)
                    for s in range(SUBS):
                        to = stage if layer else y
                        done = nc.vector.tensor_scalar(to[:, s, :], y[:, s, :], moments[:, s, 0:1],
                                                       rstd[:, s:s + 1], ALU.subtract, ALU.mult)
                    done.then_inc(normed_made, 1)
                elif step == "x1 lo" and layer == 0:
                    dve.wait_ge(x1_hi_made, b + 1)
                    nc.vector.tensor_tensor(x1_lo[:, nodes, :], y[:, :, :],
                                            x1_hi[:, nodes, :].bitcast(F32), ALU.subtract).then_inc(x1_lo_made, 1)

            def split_block(layer, b, shared, parity):
                tiles_done = tiles_before(layer, b, shared)
                for t in range(len(tile_order(layer, shared))):
                    hi_at = buffer_of(layer, b, shared, t * TILE_PIECES, HI_BUFS, TILE_PIECES)
                    step = DVE_STEPS.get(t) if before(layer, b) is not None else None
                    dve.wait_ge(hi_made, (tiles_done + (t + 1)) * TILE_PIECES)
                    if before(layer, b) is not None or t >= LO_BUFS:
                        dve.wait_ge(tile_used, tiles_done + (t - LO_BUFS + 1))
                    if step == "moments":
                        dve.wait_ge(stats_made, number(layer, b))
                    nc.vector.tensor_tensor(adj_lo[:, buffer_of(layer, b, shared, t, LO_BUFS), :],
                                            slot_of(layer, b, shared, t)[1],
                                            adj_hi[:, hi_at:hi_at + TILE_PIECES, :].bitcast(F32).rearrange("p a n -> p (a n)"),
                                            ALU.subtract).then_inc(lo_made, 1)
                    if step is not None:
                        finish(*before(layer, b), 1 - parity, step, tiles_done)
            all_blocks(dve, split_block)
            for step in DVE_STEPS.values():
                if step == "moments":
                    dve.wait_ge(stats_made, 2 * BLOCKS)
                finish(1, BLOCKS - 1, 1, step, ALL_TILES)

        @block.tensor
        def _(pe):
            pe.wait_ge(weights_in, 32)
            nc.tensor.matmul(turned[:, 0:FEAT], neigh_w[:, :], lin_w[:, 1, :], start=True, stop=True).then_inc(g_summed, 1)
            pe.wait_ge(g_shifted, 1)
            pe.wait_ge(self_made, 1)
            for c in range(H_FILLS):
                if c % QUARTER_FILLS == 0:
                    pe.wait_ge(quarter_in[c // QUARTER_FILLS], 16)
                if c >= H_BANKS:
                    pe.wait_ge(h_lo_made, c - H_BANKS + 1)
                for s in range(BANK_CHUNKS):
                    at = (c % QUARTER_FILLS) * BANK_CHUNKS * P + s * P
                    done = nc.tensor.matmul(h_ps[c % H_BANKS][:, s * 2 * FEAT:(s + 1) * 2 * FEAT],
                                            x_cols[:, c // QUARTER_FILLS, at:at + P],
                                            first_w[:, :, :].rearrange("p w f -> p (w f)"), start=True, stop=True)
                done.then_inc(h_summed, 1)
            pe.wait_ge(ones_made, 1)

            def finish(layer, b):
                n = number(layer, b)
                if layer == 0:
                    pe.wait_ge(sum_copied, b + 1)
                else:
                    pe.wait_ge(sum_added, b + 1)
                if isinstance(b, int) and b == 0 and layer == 1:
                    pe.wait_ge(agg_w_in, 16)
                if not (isinstance(b, int) and b == 0 and layer == 0):
                    pe.wait_ge(y_made, n)
                for s in range(SUBS):
                    if layer == 0:
                        done = nc.tensor.transpose(turned_v[:, s, :], sumT[:, s * P:(s + 1) * P], ident[:, :])
                    else:
                        done = nc.tensor.matmul(turned_v[:, s, :], sumT[:, s * P:(s + 1) * P], agg_w[:, :],
                                                start=True, stop=True)
                done.then_inc(turned_made, 1)

            def sum_block(layer, b, shared, parity):
                tiles_done = tiles_before(layer, b, shared)
                order = tile_order(layer, shared)
                if not isinstance(b, int) or b >= 2:
                    pe.wait_ge(sum_added if layer else sum_copied, b - 1)
                elif layer == 1:
                    pe.wait_ge(sum_copied, BLOCKS - 1 + b)
                for t, tile in enumerate(order):
                    feats = [(acc[parity], *((x1_hi, x1_lo) if layer else (h_hi, h_lo)), t == 0, t == len(order) - 1)]
                    if layer == 0 and tile < shared:
                        feats.append((acc_partial, x1_hi, x1_lo, tile == 0, tile == shared - 1))
                        if tile == 0 or tile == shared - 1:
                            pe.wait_ge(x1_lo_made, shared if tile == shared - 1 else shared - 1)
                        if tile == 0:
                            if not (isinstance(b, int) and b == FIRST_SHARING):
                                pe.wait_ge(partial_copied, b - FIRST_SHARING)
                    if layer == 1 and isinstance(b, int) and b == 0 and tile in (0, TILES - 1):
                        pe.wait_ge(x1_lo_made, BLOCKS - 1 if tile == 0 else BLOCKS)
                    for half in range(TILE_PIECES):
                        j = t * TILE_PIECES + half
                        hi_buf = buffer_of(layer, b, shared, j, HI_BUFS, TILE_PIECES)
                        chunk = tile * TILE_CHUNKS + half * PIECE_CHUNKS
                        if before(layer, b) is None:
                            pe.wait_ge(h_lo_made, (chunk + PIECE_CHUNKS) // BANK_CHUNKS)
                        pe.wait_ge(hi_made, tiles_done * TILE_PIECES + (j + 1))
                        for bank_, feat_hi, feat_lo, first, _ in feats:
                            for k in range(PIECE_CHUNKS):
                                hi = adj_hi[:, hi_buf, k * BLOCK:(k + 1) * BLOCK]
                                nc.tensor.matmul(bank_[:, :], feat_hi[:, chunk + k, :], hi,
                                                 start=(first and half + k == 0), stop=False)
                                done = nc.tensor.matmul(bank_[:, :], feat_lo[:, chunk + k, :], hi, start=False, stop=False)
                        done.then_inc(hi_used, 1)
                    pe.wait_ge(lo_made, tiles_done + (t + 1))
                    lo_buf = buffer_of(layer, b, shared, t, LO_BUFS)
                    for bank_, feat_hi, _, _, last in feats:
                        for k in range(TILE_CHUNKS):
                            done = nc.tensor.matmul(bank_[:, :], feat_hi[:, tile * TILE_CHUNKS + k, :],
                                                    adj_lo[:, lo_buf, k * BLOCK:(k + 1) * BLOCK], start=False,
                                                    stop=(last and k == TILE_CHUNKS - 1))
                    done.then_inc(tile_used, 1)
                    if t == PE_TURN and before(layer, b) is not None:
                        finish(*before(layer, b))
            all_blocks(pe, sum_block)
            finish(1, BLOCKS - 1)


ALL_TILES = sum((end - first) * (2 * TILES - shared) for first, end, shared in GROUPS)


def kernel(x, adj, L0_gnn_neigh_W, L0_gnn_lin_W, L1_gnn_w, L1_gnn_W_agg):
    import numpy as np
    import concourse.bacc as bacc
    from concourse.bass_utils import run_bass_kernel_spmd

    adj = np.asarray(adj)
    tiles = adj.reshape(BLOCKS, BLOCK, TILES, TILE_CHUNKS, P).transpose(0, 2, 4, 3, 1)
    arrays = {
        "adj_tiles": np.ascontiguousarray(tiles).reshape(BLOCKS * TILES, P, TILE_COLS),
        "xT": np.ascontiguousarray(np.asarray(x).T),
        "neigh_W": np.ascontiguousarray(L0_gnn_neigh_W),
        "lin_WT": np.ascontiguousarray(np.asarray(L0_gnn_lin_W).T.reshape(2, FEAT, FEAT).transpose(1, 0, 2)),
        "w_nodes": np.ascontiguousarray(np.asarray(L1_gnn_w).reshape(CHUNKS, P).T),
        "W_agg": np.ascontiguousarray(L1_gnn_W_agg),
    }
    nc = bacc.Bacc("TRN2", target_bir_lowering=False, num_devices=1)
    args = [nc.dram_tensor(name, a.shape, mybir.dt.from_np(a.dtype), kind="ExternalInput").ap()
            for name, a in arrays.items()]
    partials = nc.dram_tensor("partials", (BLOCKS - FIRST_SHARING, P, BLOCK), F32).ap()
    out = nc.dram_tensor("out", (P, CHUNKS, FEAT), F32, kind="ExternalOutput").ap()
    graph_two_layers(nc, *args, partials, out)
    r = run_bass_kernel_spmd(nc, [arrays], core_ids=[0])
    return np.ascontiguousarray(r.results[0]["out"].transpose(1, 0, 2)).reshape(NODES, FEAT)
```
